# Optimizing a Trainium2 kernel written in Bass

```python
import numpy as np
import jax
import jax.numpy as jnp

def _softmax(x, axis=-1):
    return jax.nn.softmax(x, axis=axis)

def _gelu(x):
    return jax.nn.gelu(x, approximate=True)

def _silu(x):
    return jax.nn.silu(x)

def _sigmoid(x):
    return jax.nn.sigmoid(x)

def _layernorm(x, axis=-1, eps=1e-05):
    m = jnp.mean(x, axis=axis, keepdims=True)
    v = jnp.var(x, axis=axis, keepdims=True)
    return (x - m) / jnp.sqrt(v + eps)

def _scatter_add(tgt, idx, src, axis=0):
    return tgt.at[idx].add(src)

def _segment_sum(src, seg, n):
    return jax.ops.segment_sum(src, seg, n)
kernel_name = 'mk_decoder_postln_d1_seqx_r2_7bffa7'

def setup_inputs(seed: int=0):
    np.random.seed(seed)
    _w = jnp.asarray

    def _rec_inputs():
        import jax
        import jax.numpy as jnp
        _rk = jax.random.key(seed)
        x = 7.22e-05 + 1 * jax.random.normal(jax.random.fold_in(_rk, 1), (8, 512, 512), jnp.float32)
        _lenS = 512 - jax.random.randint(jax.random.fold_in(_rk, 7), (8,), 0, max(1, 512 // 4) + 1, jnp.int32)
        _lenS2 = 512 - jax.random.randint(jax.random.fold_in(_rk, 8), (8,), 0, max(1, 512 // 4) + 1, jnp.int32)
        _ctx_1024P = jax.random.normal(jax.random.fold_in(_rk, 11), (8, 16, 512), jnp.float32)
        _ctx_1024c = jax.random.dirichlet(jax.random.fold_in(_rk, 511), 0.3 * jnp.ones((16,), jnp.float32), (8, 512))
        _ctx_1024t = jnp.einsum('bsk,bkd->bsd', _ctx_1024c, _ctx_1024P)
        _ctx_1024t = _ctx_1024t * jax.lax.rsqrt(jnp.mean(jnp.square(_ctx_1024t)) + 1e-12) * 0.953939
        ctx_1024 = 4.13588e-05 + 0.999923 * (_ctx_1024t + 0.3 * jax.random.normal(jax.random.fold_in(_rk, 611), (8, 512, 512), jnp.float32))
        _validS = jnp.arange(512)[None, :] < _lenS[:, None]
        _validS2 = jnp.arange(512)[None, :] < _lenS2[:, None]
        _causal = jnp.tril(jnp.ones((512, 512), dtype=bool))
        mask_1_bf0 = jnp.logical_not(jnp.ones((1,), dtype=bool))
        return (x, ctx_1024, mask_1_bf0)
    x, ctx_1024, mask_1_bf0 = _rec_inputs()

    def _L0_attn_setup():
        import jax, jax.numpy as jnp
        import numpy as np
        B, S, D, H = (4, 1024, 512, 16)
        HD = D // H

        def rope(x):
            d = x.shape[-1]
            inv_freq = 1.0 / 10000.0 ** (jnp.arange(0, d, 2, dtype=jnp.float32) / d)
            pos = jnp.arange(x.shape[1], dtype=jnp.float32)
            ang = pos[:, None] * inv_freq[None, :]
            cos, sin = (jnp.cos(ang), jnp.sin(ang))
            x1, x2 = (x[..., 0::2], x[..., 1::2])
            r1 = x1 * cos - x2 * sin
            r2 = x1 * sin + x2 * cos
            return jnp.stack([r1, r2], axis=-1).reshape(x.shape)
        key = jax.random.key(seed)
        ks = jax.random.split(key, 9)
        s = 1.0 / np.sqrt(D)

        def lin(k):
            kw, kb = jax.random.split(k)
            W = jax.random.uniform(kw, (D, D), jnp.float32, -s, s)
            b = jax.random.uniform(kb, (D,), jnp.float32, -s, s)
            return (W, b)
        Wq, bq = lin(ks[0])
        Wk, bk = lin(ks[1])
        Wv, bv = lin(ks[2])
        W0, b0 = lin(ks[3])
        x = jax.random.normal(ks[4], (B, S, D), jnp.float32)
        return {'x': x, 'Wq': Wq, 'bq': bq, 'Wk': Wk, 'bk': bk, 'Wv': Wv, 'bv': bv, 'W0': W0, 'b0': b0}
    _L0_attn_all = _L0_attn_setup()
    _L0_attn_in = {k: v for k, v in _L0_attn_all.items() if k in ('Wq', 'bq', 'Wk', 'bk', 'Wv', 'bv', 'W0', 'b0')}
    del _L0_attn_all

    def _L0_xattn_setup():
        import jax, jax.numpy as jnp
        import numpy as np
        EMBED_DIM = 512
        N_HEAD = 16
        D_K = EMBED_DIM // N_HEAD
        key = jax.random.key(seed)
        kq, kk, kv, kwq, kwk, kwv, kwo = jax.random.split(key, 7)
        B, S, E = (4, 1024, EMBED_DIM)
        scale = 1.0 / np.sqrt(E)
        return {'Q': jax.random.normal(kq, (B, S, E), dtype=jnp.float32), 'K': jax.random.normal(kk, (B, S, E), dtype=jnp.float32), 'V': jax.random.normal(kv, (B, S, E), dtype=jnp.float32), 'mask': jnp.zeros((1,), dtype=jnp.bool_), 'Wq': jax.random.normal(kwq, (E, E), dtype=jnp.float32) * scale, 'Wk': jax.random.normal(kwk, (E, E), dtype=jnp.float32) * scale, 'Wv': jax.random.normal(kwv, (E, E), dtype=jnp.float32) * scale, 'Wo': jax.random.normal(kwo, (E, E), dtype=jnp.float32) * scale}
    _L0_xattn_all = _L0_xattn_setup()
    _L0_xattn_in = {k: v for k, v in _L0_xattn_all.items() if k in ('Wq', 'Wk', 'Wv', 'Wo')}
    del _L0_xattn_all

    def _L0_ffn_setup():
        import jax, jax.numpy as jnp
        import numpy as np
        D_MODEL = 512
        M = 64
        INNER = 16
        key = jax.random.key(seed)
        ks = jax.random.split(key, 9)

        def init(k, shape, fan_in):
            bound = 1.0 / np.sqrt(fan_in)
            return jax.random.uniform(k, shape, jnp.float32, -bound, bound)
        x = jax.random.normal(ks[0], (16, 2048, D_MODEL), dtype=jnp.float32)
        Win = init(ks[1], (D_MODEL, M), D_MODEL)
        bin_ = init(ks[2], (M,), D_MODEL)
        W1 = init(ks[3], (M, INNER), 1)
        b1 = init(ks[4], (M, INNER), 1)
        W2 = init(ks[5], (M, INNER), INNER)
        b2 = init(ks[6], (M,), INNER)
        Wout = init(ks[7], (M, D_MODEL), M)
        bout = init(ks[8], (D_MODEL,), M)
        return {'x': x, 'Win': Win, 'bin_': bin_, 'W1': W1, 'b1': b1, 'W2': W2, 'b2': b2, 'Wout': Wout, 'bout': bout}
    _L0_ffn_all = _L0_ffn_setup()
    _L0_ffn_in = {k: v for k, v in _L0_ffn_all.items() if k in ('Win', 'bin_', 'W1', 'b1', 'W2', 'b2', 'Wout', 'bout')}
    del _L0_ffn_all
    return {'x': x, 'ctx_1024': ctx_1024, 'mask_1_bf0': mask_1_bf0, 'L0_attn_Wq': _L0_attn_in['Wq'], 'L0_attn_bq': _L0_attn_in['bq'], 'L0_attn_Wk': _L0_attn_in['Wk'], 'L0_attn_bk': _L0_attn_in['bk'], 'L0_attn_Wv': _L0_attn_in['Wv'], 'L0_attn_bv': _L0_attn_in['bv'], 'L0_attn_W0': _L0_attn_in['W0'], 'L0_attn_b0': _L0_attn_in['b0'], 'L0_xattn_Wq': _L0_xattn_in['Wq'], 'L0_xattn_Wk': _L0_xattn_in['Wk'], 'L0_xattn_Wv': _L0_xattn_in['Wv'], 'L0_xattn_Wo': _L0_xattn_in['Wo'], 'L0_ffn_Win': _L0_ffn_in['Win'], 'L0_ffn_bin_': _L0_ffn_in['bin_'], 'L0_ffn_W1': _L0_ffn_in['W1'], 'L0_ffn_b1': _L0_ffn_in['b1'], 'L0_ffn_W2': _L0_ffn_in['W2'], 'L0_ffn_b2': _L0_ffn_in['b2'], 'L0_ffn_Wout': _L0_ffn_in['Wout'], 'L0_ffn_bout': _L0_ffn_in['bout']}

def reference(x, ctx_1024, mask_1_bf0, L0_attn_Wq, L0_attn_bq, L0_attn_Wk, L0_attn_bk, L0_attn_Wv, L0_attn_bv, L0_attn_W0, L0_attn_b0, L0_xattn_Wq, L0_xattn_Wk, L0_xattn_Wv, L0_xattn_Wo, L0_ffn_Win, L0_ffn_bin_, L0_ffn_W1, L0_ffn_b1, L0_ffn_W2, L0_ffn_b2, L0_ffn_Wout, L0_ffn_bout):
    import jax
    import jax.numpy as jnp

    def _L0_attn_ref(x, Wq, bq, Wk, bk, Wv, bv, W0, b0):
        import jax, jax.numpy as jnp
        import numpy as np
        B, S, D, H = (4, 1024, 512, 16)
        HD = D // H

        def rope(x):
            d = x.shape[-1]
            inv_freq = 1.0 / 10000.0 ** (jnp.arange(0, d, 2, dtype=jnp.float32) / d)
            pos = jnp.arange(x.shape[1], dtype=jnp.float32)
            ang = pos[:, None] * inv_freq[None, :]
            cos, sin = (jnp.cos(ang), jnp.sin(ang))
            x1, x2 = (x[..., 0::2], x[..., 1::2])
            r1 = x1 * cos - x2 * sin
            r2 = x1 * sin + x2 * cos
            return jnp.stack([r1, r2], axis=-1).reshape(x.shape)
        q = x @ Wq + bq
        k = x @ Wk + bk
        v = x @ Wv + bv
        q = rope(q)
        k = rope(k)
        b, s, _ = x.shape
        qh = q.reshape(b, s, H, HD).transpose(0, 2, 1, 3)
        kh = k.reshape(b, s, H, HD).transpose(0, 2, 1, 3)
        vh = v.reshape(b, s, H, HD).transpose(0, 2, 1, 3)
        scores = jnp.einsum('bhqd,bhkd->bhqk', qh, kh) / jnp.sqrt(jnp.float32(HD))
        attn = jax.nn.softmax(scores, axis=-1)
        out = jnp.einsum('bhqk,bhkd->bhqd', attn, vh)
        out = out.transpose(0, 2, 1, 3).reshape(b, s, D)
        return out @ W0 + b0

    def _L0_xattn_ref(Q, K, V, mask, Wq, Wk, Wv, Wo):
        import jax, jax.numpy as jnp
        import numpy as np
        EMBED_DIM = 512
        N_HEAD = 16
        D_K = EMBED_DIM // N_HEAD
        B, S, E = Q.shape
        H, Dk = (N_HEAD, D_K)
        q = (Q @ Wq.T).reshape(B, S, H, Dk).transpose(0, 2, 1, 3)
        k = (K @ Wk.T).reshape(B, S, H, Dk).transpose(0, 2, 1, 3)
        v = (V @ Wv.T).reshape(B, S, H, Dk).transpose(0, 2, 1, 3)
        scores = jnp.einsum('bhqd,bhkd->bhqk', q, k) / jnp.sqrt(jnp.float32(Dk))
        attn = jax.nn.softmax(scores, axis=-1)
        ctx = jnp.einsum('bhqk,bhkd->bhqd', attn, v)
        ctx = ctx.transpose(0, 2, 1, 3).reshape(B, S, E)
        return ctx @ Wo.T

    def _L0_ffn_ref(x, Win, bin_, W1, b1, W2, b2, Wout, bout):
        import jax, jax.numpy as jnp
        import numpy as np
        D_MODEL = 512
        M = 64
        INNER = 16
        s = jnp.einsum('btd,dm->btm', x, Win) + bin_
        h = jax.nn.relu(s[..., None] * W1 + b1)
        g = jnp.einsum('btmh,mh->btm', h, W2) + b2
        out = jnp.einsum('btm,md->btd', g, Wout) + bout
        return out
    x = _layernorm(x + _L0_attn_ref(x, L0_attn_Wq, L0_attn_bq, L0_attn_Wk, L0_attn_bk, L0_attn_Wv, L0_attn_bv, L0_attn_W0, L0_attn_b0), axis=-1)
    x = _layernorm(x + _L0_xattn_ref(x, ctx_1024, ctx_1024, mask_1_bf0, L0_xattn_Wq, L0_xattn_Wk, L0_xattn_Wv, L0_xattn_Wo), axis=-1)
    x = _layernorm(x + _L0_ffn_ref(x, L0_ffn_Win, L0_ffn_bin_, L0_ffn_W1, L0_ffn_b1, L0_ffn_W2, L0_ffn_b2, L0_ffn_Wout, L0_ffn_bout), axis=-1)
    return x

_drawn_inputs = setup_inputs


def setup_inputs(seed=0):
    import zlib

    import numpy as np

    out = dict(_drawn_inputs(seed))
    spreads = {}
    factors = {'L0_attn_Wq': 8.0,
     'L0_attn_bq': 8.0,
     'L0_attn_Wk': 8.0,
     'L0_attn_bk': 8.0,
     'L0_attn_Wv': 4.022,
     'L0_attn_bv': 4.167,
     'L0_attn_W0': 2.906,
     'L0_ffn_bin_': 8.0,
     'L0_attn_b0': 8.0}
    for name, (base, spread) in spreads.items():
        noise = np.random.default_rng([zlib.crc32(name.encode()), seed]).standard_normal(out[name].shape)
        drawn = base * np.exp(spread * noise) if base else spread * noise
        out[name] = jnp.asarray(drawn.astype(out[name].dtype))
    for name, factor in factors.items():
        out[name] = (out[name] * factor).astype(out[name].dtype)
    return out
```

```python
from contextlib import ExitStack

import concourse.bass as bass
import numpy as np
from concourse import mybir
from concourse.alu_op_type import AluOpType as ALU

F32 = mybir.dt.float32
F32R = mybir.dt.float32r
ACT = mybir.ActivationFunctionType
AX = mybir.AxisListType

B, S, D = 8, 512, 512
H = 16
HD = D // H
P = 128
KT = D // P
QT = S // P
NGRP = 4
NC = 4
STEPS = NGRP * KT
LEAD = 6
EPS = 1e-5
M, INNER = 64, 16
FT = M * INNER // P


class At:

    def __init__(self, counts, b=None):
        self.counts, self.b = counts, b

    def __call__(self, name, k):
        before, each = self.counts[name]
        return k if self.b is None else self.b * each + (before + k)


def ring_order(items):
    return {item: n for n, item in enumerate(items)}


def max_slots(s):
    return [("max", s, qt) for qt in range(QT)]


def attention_layer(nc, rope, source, second, resid, weights, out_dram, sums_dram):
    wq_d, wk_d, wv_d, wo_d, bq_d, bk_d, bv_d, bo_d, table_d = weights
    SCALE = float(HD) ** -0.5

    NG, NX = 3, 3
    proj = [("q", u) for u in range(KT)]
    kproj = [("k", u) for u in range(KT)]
    vproj = [("v", t) for t in range(QT)]
    scores = [("score", n, c) for n in range(STEPS) for c in range(NC)]
    G0 = ring_order(proj + kproj + vproj)
    G1 = ring_order(scores + proj + kproj + vproj)
    outs = [("out", t) for t in range(QT)]
    lead = []
    for s in range(LEAD):
        lead += max_slots(s)[:2] + ([("mt", 0)] if s == 4 else []) + max_slots(s)[2:]
    turn = [] if rope else [("turn", t) for t in range(QT)]
    att = []
    turned = {NC * a + NC - LEAD: a for a in range(1, NGRP)}
    for n in range(STEPS):
        s = n + LEAD
        ms = max_slots(s) if s < H else []
        att += ms[:2] + ([("mt", turned[n])] if n in turned else []) + ms[2:]
    X0 = ring_order(turn + lead)
    X1 = ring_order(att + turn + outs + lead)
    X2 = ring_order(att + outs)
    COUNTS = {
        "g": (len(G0), len(G1)), "x": (len(X0), len(X1)), "p_used": (0, STEPS), "acc": (0, 2 * H),
        "group": (0, NGRP), "group_dma": (0, 16 * NGRP), "negmax": (1, NGRP), "max_rows": (32, 32 * NGRP),
        "stack": (96, 96), "split": (KT, KT), "unit": (2 * KT, 2 * KT), "stage": (32, 32), "dma": (16, 16),
        "tile": (0, QT), "tile_dma": (0, 16), "ln_small": (0, 4 * QT),
    }

    ctx = ExitStack()
    with ctx:
        def sb(name, shape, dt=F32):
            return ctx.enter_context(nc.sbuf_tensor(("self_" if rope else "cross_") + name, shape, dt))

        def sem(name):
            return ctx.enter_context(nc.semaphore(("self_" if rope else "cross_") + name))

        Wh = [sb(f"w{n}_hi", [P, KT, D], F32R) for n in "qkv"]
        Wl = [sb(f"w{n}_lo", [P, KT, D], F32R) for n in "qkv"]
        Wo = sb("wo", [P, NGRP, D])
        qstk = sb("q_stack", [P, H, S], F32R)
        kstk = sb("k_stack", [P, H, S], F32R)
        xh = sb("x_hi", [P, KT, S], F32R)
        xl = sb("x_lo", [P, KT, S], F32R)
        O = sb("o", [P, NGRP, S])
        V = sb("v", [P, QT, D])
        prob = sb("prob", [P, 3, NC, S])
        part_hi, part_lo, work = prob[:, 0], prob[:, 1], prob[:, 2]
        acc = sb("acc", [P, NC, S])
        table0 = sb("table0", [P, 2, S]) if rope else None
        stage = sb("stage", [P, 2, S])
        tables = (table0, stage[:, :], acc[:, 2:4], acc[:, 0:2])
        res = sb("res", [P, QT, D])
        rsum = sb("rsum", [P, 16])
        sums = sb("sums", [P, S])
        bo = sb("bo", [P, D])
        ident = sb("ident", [P, P])
        ones = sb("ones", [P, 32])
        half, minus, eps = sb("neg_half", [P, 1]), sb("minus_one", [P, 1]), sb("eps", [P, 1])
        bqk = sb("bqk", [P, 2, KT])
        bv = sb("bv", [P, NGRP])
        pause = sb("pause", [P, 2])
        mx = sb("mx", [P, 2, NC * QT])
        negm = sb("negm", [16, P])
        negm_hl = sb("negm_hl", [16, 2, P], F32R)
        st = sb("bn_stats", [P, 6])
        mv = sb("bn_mv", [P, QT, 2])
        lns = sb("ln_small", [P, QT, 4])

        G = [ctx.enter_context(nc.psum_tensor(f"{'self' if rope else 'cross'}_g{i}", [P, 512], F32)) for i in range(NG)]
        X = [ctx.enter_context(nc.psum_tensor(f"{'self' if rope else 'cross'}_x{i}", [P, 512], F32)) for i in range(NX)]
        OP = ctx.enter_context(nc.psum_tensor(f"{'self' if rope else 'cross'}_o_acc", [P, 512], F32))
        SP_ = ctx.enter_context(nc.psum_tensor(f"{'self' if rope else 'cross'}_s_acc", [P, 512], F32))

        w_in = [sem(f"w_in{i}") for i in range(3)]
        small_in, wo_in = sem("small_in"), sem("wo_in")
        w_hi, w_lo = sem("w_hi"), sem("w_lo")
        ones_rows = sem("ones_rows")
        const_ready, bo_sum, bo_ready, bvb_ready, bvo_copied = (
            sem("const_ready"), sem("bo_sum"), sem("bo_ready"), sem("bvb_ready"), sem("bvo_copied"))
        stage_in = [sem("stage_in0"), sem("stage_in1")]
        table_in = [sem(f"table_in{t}") for t in range(KT)]
        ctx_in = sem("ctx_in")
        x_split = sem("x_split")
        g_full, g_evac = sem("g_full"), sem("g_evac")
        x_full, x_done = sem("x_full"), sem("x_done")
        swapped, cos_done, sin_done, unit_split = sem("swapped"), sem("cos_done"), sem("sin_done"), sem("unit_split")
        stack_in = [[sem(f"stack_in{h}_{a}") for a in range(NGRP)] for h in range(2)]
        negmax_ready, max_rows_in = sem("negmax_ready"), sem("max_rows_in")
        p_used, acc_added = sem("p_used"), sem("acc_added")
        o_full, o_copied, s_full, s_copied = sem("o_full"), sem("o_copied"), sem("s_full"), sem("s_copied")
        spread_in, recip_done, recip_out, sums_in, o_ready = (
            sem("spread_in"), sem("recip_done"), sem("recip_out"), sem("sums_in"), sem("o_ready"))
        res_in = [sem(f"res_in{t}") for t in range(QT)]
        y_out = [sem(f"y_out{t}") for t in range(QT)]
        bias_added, ln_stats, ln_small, ln_out = sem("bias_added"), sem("ln_stats"), sem("ln_small"), sem("ln_out")
        dve_seq = sem("dve_seq")

        def wait_table(eng, at, u):
            t = u % KT
            eng.wait_ge(table_in[t], 16 if t == 0 else at("dma", 16))

        block = ctx.enter_context(nc.Block())

        @block.sync
        def _(sp):
            for i, w in enumerate((wq_d, wk_d, wv_d)):
                sp.dma_start(prob[:, i], w).then_inc(w_in[i], 16)
                if i == 0:
                    for t in range(2):
                        sp.dma_start(stage[:, t], source[0, t]).then_inc(stage_in[t], 16)
            if rope:
                sp.dma_start(bqk[:, 0], bq_d).then_inc(small_in, 16)
                sp.dma_start(bqk[:, 1], bk_d).then_inc(small_in, 16)
                sp.dma_start(bv[:, :], bv_d).then_inc(small_in, 16)
                sp.dma_start(bo[:, :], bo_d).then_inc(small_in, 16)

            def load_stage(at, b, t):
                if rope and t < 2:
                    sp.wait_ge(unit_split, at("unit", 0))
                elif rope:
                    sp.wait_ge(x_split, at("split", max(t - 1, 0)))
                elif t < 2:
                    sp.wait_ge(x_full, at("x", 0))
                else:
                    sp.wait_ge(x_full, at("x", (X0 if at.b is None else X1)[("turn", t - 2)] + 1))
                sp.dma_start(stage[:, t % 2], source[b, t]).then_inc(stage_in[t % 2], 16)

            def load_table(at, t):
                sp.dma_start(tables[t], table_d[t]).then_inc(table_in[t], 16)

            def stacks(at, which, half):
                sp.wait_ge(unit_split, at("unit", KT * which + 2 * (half + 1)))
                dst = (qstk, kstk)[which]
                parts = ((part_hi, part_hi, part_lo), (part_hi, part_lo, part_hi))[which]
                for a in range(NGRP):
                    for r, part in enumerate(parts):
                        sp.dma_start(dst[32 * r:32 * r + 32, 4 * a + 2 * half:4 * a + 2 * half + 2, :].bitcast(F32),
                                     part[32 * a:32 * a + 32, 2 * half:2 * half + 2]).then_inc(stack_in[half][a], 16)

            def max_rows(at, a, k):
                sp.wait_ge(negmax_ready, at("negmax", k))
                for r in range(2):
                    sp.dma_start(qstk[96 + r:97 + r, 4 * a:4 * a + 4, :].bitcast(F32),
                                 negm_hl[:, r, :].bitcast(F32)).then_inc(max_rows_in, 16)

            def spread(at, g):
                sp.wait_ge(s_copied, at("group", g + 1))
                sp.dma_start(rsum[:, :], sums[0:P:32, :]).then_inc(spread_in, 16)

            def recip_store(at, g):
                sp.wait_ge(recip_done, at("group", g + 1))
                sp.dma_start(sums_dram[g].rearrange("c (b t) -> (c b) t", t=16), rsum[:, :]).then_inc(recip_out, 16)

            def recip_load(at, g):
                sp.wait_ge(recip_out, at("group_dma", 16 * (g + 1)))
                src = bass.AP(sums_dram.tensor, g * NC * S, [[S, NC], [0, 32], [1, S]])
                sp.dma_start(sums[:, :], src).then_inc(sums_in, 16)

            def load_res(b, t):
                sp.dma_start(res[:, t], resid[b, t]).then_inc(res_in[t], 16)

            def store(at, b, t):
                sp.wait_ge(ln_out, at("tile", t + 1))
                sp.dma_start(out_dram[b, t], res[:, t]).then_inc(y_out[t], 16)

            def attention(at, b, last):
                if not last:
                    for t in range(2):
                        load_stage(at, b + 1, t)
                max_rows(at, 1, 1)
                spread(at, 0)
                max_rows(at, 2, 2)
                recip_store(at, 0)
                recip_load(at, 0)
                spread(at, 1)
                max_rows(at, 3, 3)
                recip_store(at, 1)
                recip_load(at, 1)
                if not last:
                    for t in range(2, 4):
                        load_stage(at, b + 1, t)
                spread(at, 2)
                recip_store(at, 2)
                recip_load(at, 2)

            def project(at, b, first):
                if rope:
                    sp.wait_ge(x_split, at("split", KT))
                    load_table(at, 1)
                if not first:
                    sp.wait_ge(s_full, at("group", NGRP))
                if rope:
                    load_table(at, 2)
                    load_table(at, 3)
                else:
                    sp.dma_start(acc[:, :, :], second[b]).then_inc(ctx_in, 16)
                if not first:
                    spread(at, 3)
                    recip_store(at, 3)
                    recip_load(at, 3)
                stacks(at, 0, 0)
                stacks(at, 0, 1)
                stacks(at, 1, 0)
                stacks(at, 1, 1)
                if not first:
                    store(at, b - 1, 0)
                    store(at, b - 1, 1)
                max_rows(at, 0, 1 if first else NGRP)
                if not first:
                    store(at, b - 1, 2)
                    store(at, b - 1, 3)
                for t in range(QT):
                    if not first:
                        sp.wait_ge(y_out[t], at("tile_dma", 16))
                    load_res(b, t)

            at = At(COUNTS)
            for t in range(2, 4):
                load_stage(at, 0, t)
            if rope:
                sp.dma_start(table0[:, :, :], table_d[0]).then_inc(table_in[0], 16)
            sp.dma_start(Wo[:, :, :], wo_d).then_inc(wo_in, 16)
            sp.wait_ge(w_lo, 3)
            project(at, 0, True)
            with sp.Fori(0, B - 1) as b:
                at = At(COUNTS, b)
                attention(at, b, False)
                project(at, b + 1, False)
            at, b = At(COUNTS, B - 1), B - 1
            attention(at, b, True)
            spread(at, 3)
            recip_store(at, 3)
            recip_load(at, 3)
            for t in range(QT):
                store(at, b, t)
            for t in range(QT):
                sp.wait_ge(y_out[t], at("tile_dma", 16))

        @block.gpsimd
        def _(pool):
            pool.memset(ident[:, :], 0.0).then_inc(const_ready, 1)
            pool.memset(ones[:, :], 1.0).then_inc(const_ready, 1)
            pool.memset(half[:, :], -0.5).then_inc(const_ready, 1)
            pool.memset(minus[:, :], -1.0).then_inc(const_ready, 1)
            pool.memset(eps[:, :], EPS).then_inc(const_ready, 1)
            pool.wait_ge(const_ready, 5)
            pool.affine_select(out=ident[:, :], in_=ident[:, :], compare_op=ALU.not_equal, fill=1.0,
                               base=0, pattern=[[-1, P]], channel_multiplier=1).then_inc(const_ready, 1)
            pool.wait_ge(const_ready, 6)
            pool.memset(kstk[96:128, :, :].bitcast(F32), 1.0).then_inc(ones_rows, 1)

            pool.wait_ge(ones_rows, 1)

            def unit_products(at, u):
                wait_table(pool, at, u)
                pool.wait_ge(swapped, at("unit", u + 1))
                w, w2 = work[:, 2 * (u % 2)], work[:, 2 * (u % 2) + 1]
                pool.tensor_tensor(w, w, tables[u % KT][:, 0], ALU.mult).then_inc(cos_done, 1)
                pool.tensor_tensor(w2, w2, tables[u % KT][:, 1], ALU.mult).then_inc(sin_done, 1)

            def add_bias(at, t):
                pool.wait_ge(res_in[t], at("tile_dma", 16))
                pool.tensor_tensor(res[:, t], res[:, t], bo[:, :], ALU.add).then_inc(bias_added, 1)

            def ln_scalars(at, t):
                s, m = lns[:, t], mv[:, t]
                k = 4 * t
                pool.wait_ge(ln_stats, at("tile", t + 1))
                pool.tensor_tensor(s[:, 0:1], m[:, 1:2], eps[:, :], ALU.add).then_inc(ln_small, 1)
                pool.tensor_tensor(s[:, 1:2], m[:, 0:1], minus[:, :], ALU.mult).then_inc(ln_small, 1)
                pool.wait_ge(ln_small, at("ln_small", k + 2))
                pool.tensor_tensor(s[:, 2:3], s[:, 0:1], half[:, :], ALU.pow).then_inc(ln_small, 1)
                pool.wait_ge(ln_small, at("ln_small", k + 3))
                pool.tensor_tensor(s[:, 3:4], s[:, 1:2], s[:, 2:3], ALU.mult).then_inc(ln_small, 1)

            def attention(at):
                for g in range(NGRP):
                    for c in range(NC):
                        for kt in (0, 1):
                            pool.wait_ge(g_evac, at("g", G1[("score", KT * g + kt, c)] + 1))
                        if c == 0 and g > 0:
                            pool.wait_ge(s_full, at("group", g))
                        pool.tensor_tensor(acc[:, c], prob[:, (KT * g) % 3, c], prob[:, (KT * g + 1) % 3, c],
                                           ALU.add).then_inc(acc_added, 1)
                    for c in range(NC):
                        pool.wait_ge(g_evac, at("g", G1[("score", KT * g + 2, c)] + 1))
                        pool.wait_ge(acc_added, at("acc", 8 * g + c + 1))
                        pool.tensor_tensor(acc[:, c], acc[:, c], prob[:, (KT * g + 2) % 3, c],
                                           ALU.add).then_inc(acc_added, 1)
                    if rope:
                        add_bias(at, g)

            def project(at, first):
                for u in range(2 * KT):
                    if rope:
                        unit_products(at, u)
                    if u == KT + 2 and not first:
                        ln_scalars(at, 0)
                if not first:
                    for t in range(1, QT):
                        ln_scalars(at, t)

            def acc_free(at):
                if rope:
                    pool.wait_ge(unit_split, at("unit", 2 * KT))
                else:
                    pool.wait_ge(x_split, at("split", KT))

            at = At(COUNTS)
            project(at, True)
            if rope:
                pool.wait_ge(small_in, 64)
                pool.wait_ge(bvo_copied, 1)
                pool.tensor_tensor(bo[:, :], bo[:, :], sums[:, :], ALU.add).then_inc(bo_ready, 1)
                pool.wait_ge(bo_ready, 1)
            acc_free(at)
            with pool.Fori(0, B - 1) as b:
                at = At(COUNTS, b)
                attention(at)
                project(at, False)
                acc_free(at)
            at = At(COUNTS, B - 1)
            attention(at)
            for t in range(QT):
                ln_scalars(at, t)

        @block.scalar
        def _(act):
            for i in range(3):
                act.wait_ge(w_in[i], 16)
                act.activation(Wh[i][:, :, :], prob[:, i], ACT.Identity).then_inc(w_hi, 1)

            def wait_g(at, k):
                act.wait_ge(g_full, at("g", k + 1))

            def unit(at, u, k):
                wait_g(at, k)
                if u >= 2:
                    act.wait_ge(unit_split, at("unit", u - 1))
                dst = work[:, 2 * (u % 2)]
                bias = bqk[:, u // KT, u % KT:u % KT + 1] if rope else 0.0
                act.activation(dst, G[k % NG][:, :], ACT.Identity, bias=bias).then_inc(g_evac, 1)

            def values(at, t, k):
                wait_g(at, k)
                act.activation(V[:, t], G[k % NG][:, :], ACT.Copy).then_inc(g_evac, 1)

            def normalised(at, t):
                act.wait_ge(ln_small, at("ln_small", 4 * t + 4))
                act.activation(res[:, t], res[:, t], ACT.Identity, bias=lns[:, t, 3:4],
                               scale=lns[:, t, 2:3]).then_inc(ln_out, 1)

            def copy_o(at, g):
                act.wait_ge(o_full, at("group", g + 1))
                act.activation(O[:, g], OP[:, :], ACT.Copy).then_inc(o_copied, 1)

            def copy_s(at, g):
                act.wait_ge(s_full, at("group", g + 1))
                if g:
                    act.wait_ge(o_ready, at("group", g))
                act.activation(sums[:, :], SP_[:, :], ACT.Copy).then_inc(s_copied, 1)

            def attention(at):
                for half in stack_in:
                    for a in range(NGRP):
                        act.wait_ge(half[a], at("stack", 0))
                for n in range(STEPS):
                    for c in range(NC):
                        k = G1[("score", n, c)]
                        wait_g(at, k)
                        if n >= 3:
                            if c == 0:
                                act.wait_ge(p_used, at("p_used", n - 2))
                            g, kt = divmod(n - 3, KT)
                            if kt < 3:
                                act.wait_ge(acc_added, at("acc", 8 * g + (4 if kt == 2 else 0) + c + 1))
                        act.activation(prob[:, n % 3, c], G[k % NG][:, :], ACT.Exp, scale=SCALE).then_inc(g_evac, 1)
                        if c == 3 and n % KT == 0 and n > 0:
                            copy_o(at, n // KT - 1)
                        if c == 1 and n % KT == 2 and n > 4:
                            copy_s(at, n // KT - 1)

            def project(at, first, order):
                if not first:
                    copy_o(at, 3)
                    act.wait_ge(p_used, at("p_used", STEPS))
                    act.wait_ge(acc_added, at("acc", 2 * H))
                unit(at, 0, order[("q", 0)])
                if not first:
                    copy_s(at, 3)
                for u in range(1, KT):
                    unit(at, u, order[("q", u)])
                for u in range(KT):
                    unit(at, KT + u, order[("k", u)])
                if not first:
                    normalised(at, 0)
                for t in range(QT):
                    values(at, t, order[("v", t)])
                    if not first and t < QT - 1:
                        normalised(at, 1 + t)

            at = At(COUNTS)
            act.wait_ge(w_lo, 3)
            if rope:
                act.wait_ge(small_in, 64)
            project(at, True, G0)
            if rope:
                act.wait_ge(bo_sum, 1)
                act.activation(sums[:, :], SP_[:, :], ACT.Copy).then_inc(bvo_copied, 1)
            with act.Fori(0, B - 1) as b:
                at = At(COUNTS, b)
                attention(at)
                project(at, False, G1)
            at = At(COUNTS, B - 1)
            attention(at)
            copy_o(at, 3)
            copy_s(at, 3)
            for t in range(QT):
                normalised(at, t)

        @block.vector
        def _(dve):
            seq = [0]

            def link(ins):
                ins.then_inc(dve_seq, 1)
                seq[0] += 1
                dve.wait_ge(dve_seq, seq[0])

            def restart():
                dve.sem_clear(dve_seq)
                seq[0] = 0

            def split_self(at, t):
                dve.wait_ge(stage_in[t % 2], at("stage", 16 * (t // 2 + 1)))
                link(dve.tensor_copy(xh[:, t], stage[:, t % 2]))
                dve.tensor_tensor(xl[:, t], stage[:, t % 2], xh[:, t], ALU.subtract).then_inc(x_split, 1)

            def split_turned(at, t, k):
                dve.wait_ge(x_full, at("x", k + 1))
                src = X[k % NX][:, :].rearrange("p (k t) -> p k t", k=KT)
                hi, lo = xh[:, :, P * t:P * t + P], xl[:, :, P * t:P * t + P]
                link(dve.tensor_copy(hi, src))
                dve.tensor_tensor(lo, src, hi, ALU.subtract).then_inc(x_done, 1)

            if rope:
                link(dve.memset(pause[:, :], 0.0))
            for i in range(3):
                dve.wait_ge(w_hi, i + 1)
                dve.tensor_tensor(Wl[i][:, :, :], prob[:, i], Wh[i][:, :, :], ALU.subtract).then_inc(w_lo, 1)
                if i == 0:
                    for t in range(4):
                        if rope:
                            split_self(At(COUNTS), t)
                        else:
                            split_turned(At(COUNTS), t, X0[("turn", t)])
                if i == 2 and rope:
                    dve.wait_ge(small_in, 64)
                    dve.wait_ge(const_ready, 6)
                    for a in range(NGRP):
                        dve.tensor_scalar(O[:, a, 0:P], ident[:, :], 0.0, bv[:, a:a + 1],
                                          ALU.mult, ALU.add).then_inc(bvb_ready, 1)

            def split_context(at, t):
                if t == 0:
                    dve.wait_ge(ctx_in, at("dma", 16))
                link(dve.tensor_copy(xh[:, t], acc[:, t]))
                dve.tensor_tensor(xl[:, t], acc[:, t], xh[:, t], ALU.subtract).then_inc(x_split, 1)

            def swap(at, u, k):
                if rope:
                    dve.wait_ge(g_evac, at("g", k + 1))
                    w, w2 = work[:, 2 * (u % 2)], work[:, 2 * (u % 2) + 1]
                    link(dve.tensor_copy(pause[:, 1:2], pause[:, 0:1]))
                    dve.stream_shuffle(w2, w, [i ^ 1 for i in range(32)]).then_inc(swapped, 1)

            def split(at, u, k):
                mt = u % KT
                w, w2 = work[:, 2 * (u % 2)], work[:, 2 * (u % 2) + 1]
                if rope:
                    dve.wait_ge(cos_done, at("unit", u + 1))
                    dve.wait_ge(sin_done, at("unit", u + 1))
                    link(dve.tensor_tensor(w, w, w2, ALU.add))
                else:
                    dve.wait_ge(g_evac, at("g", k + 1))
                if u in (KT, KT + 2):
                    for a in range(NGRP):
                        dve.wait_ge(stack_in[(u - KT) // 2][a], at("stack", 48))
                link(dve.tensor_copy(part_hi[:, mt].bitcast(F32R), w))
                dve.tensor_tensor(part_lo[:, mt].bitcast(F32R), w, part_hi[:, mt].bitcast(F32R),
                                  ALU.subtract).then_inc(unit_split, 1)

            def reduce(at, k, s, qt):
                a, c = divmod(s, NC)
                dve.wait_ge(x_full, at("x", k + 1))
                dve.reduce_max(mx[:, a % 2, 4 * c + qt:4 * c + qt + 1], X[k % NX][:, :], AX.X).then_inc(x_done, 1)

            def negate(at, k, n):
                dve.wait_ge(x_full, at("x", k + 1))
                if at.b is not None or n > 1:
                    dve.wait_ge(max_rows_in, at("max_rows", 32 * (n - 1)))
                dve.tensor_scalar(negm[:, :], X[k % NX][0:16, 0:P], -1.0, None, ALU.mult).then_inc(x_done, 1)
                dve.wait_ge(x_done, at("x", k + 1))
                link(dve.tensor_copy(negm_hl[:, 0], negm[:, :]))
                dve.tensor_tensor(negm_hl[:, 1], negm[:, :], negm_hl[:, 0], ALU.subtract).then_inc(negmax_ready, 1)

            def recip(at, g):
                dve.wait_ge(spread_in, at("group_dma", 16 * (g + 1)))
                dve.reciprocal(rsum[:, :], rsum[:, :]).then_inc(recip_done, 1)

            def scale_o(at, g):
                dve.wait_ge(sums_in, at("group_dma", 16 * (g + 1)))
                dve.wait_ge(o_copied, at("group", g + 1))
                dve.tensor_tensor(O[:, g], O[:, g], sums[:, :], ALU.mult).then_inc(o_ready, 1)

            def output(at, t, k):
                if t:
                    dve.wait_ge(ln_stats, at("tile", t))
                if rope:
                    dve.wait_ge(bias_added, at("tile", t + 1))
                else:
                    dve.wait_ge(res_in[t], at("tile_dma", 16))
                dve.wait_ge(x_full, at("x", k + 1))
                dve.tensor_tensor(res[:, t], X[k % NX][:, :], res[:, t], ALU.add).then_inc(x_done, 1)
                dve.wait_ge(x_done, at("x", k + 1))
                link(dve.bn_stats(st[:, :], res[:, t]))
                dve.bn_aggr(mv[:, t], st[:, :]).then_inc(ln_stats, 1)

            def attention(at, last):
                order = X2 if last else X1
                for n in range(STEPS):
                    s = n + LEAD
                    for qt in range(QT):
                        if s < H:
                            reduce(at, order[("max", s, qt)], s, qt)
                        if qt == 1:
                            if n in turned:
                                negate(at, order[("mt", turned[n])], turned[n])
                            if n in (7, 11, 15):
                                recip(at, n // 4 - 1)
                            if n in (9, 13):
                                scale_o(at, n // 4 - 2)
                    if n in (11, 12, 13, 14) and not last:
                        t = n - 11
                        if rope:
                            split_self(at, t)
                        else:
                            split_turned(at, t, order[("turn", t)])
                scale_o(at, 2)

            def project(at, first, order, xorder):
                swap(at, 0, order[("q", 0)])
                swap(at, 1, order[("q", 1)])
                split(at, 0, order[("q", 0)])
                if not first:
                    recip(at, 3)
                swap(at, 2, order[("q", 2)])
                split(at, 1, order[("q", 1)])
                swap(at, 3, order[("q", 3)])
                if not rope:
                    dve.wait_ge(g_evac, at("g", order[("q", 3)] + 1))
                    for t in range(KT):
                        split_context(at, t)
                split(at, 2, order[("q", 2)])
                if not first:
                    scale_o(at, 3)
                swap(at, KT, order[("k", 0)])
                split(at, 3, order[("q", 3)])
                swap(at, KT + 1, order[("k", 1)])
                if not first:
                    output(at, 0, xorder[("out", 0)])
                split(at, KT, order[("k", 0)])
                swap(at, KT + 2, order[("k", 2)])
                split(at, KT + 1, order[("k", 1)])
                swap(at, KT + 3, order[("k", 3)])
                split(at, KT + 2, order[("k", 2)])
                split(at, KT + 3, order[("k", 3)])
                if not first:
                    output(at, 1, xorder[("out", 1)])
                    output(at, 2, xorder[("out", 2)])
                    output(at, 3, xorder[("out", 3)])
                for s in range(LEAD):
                    for qt in range(QT):
                        reduce(at, xorder[("max", s, qt)], s, qt)
                        if s == 4 and qt == 1:
                            negate(at, xorder[("mt", 0)], 1 if first else NGRP)

            project(At(COUNTS), True, G0, X0)
            with dve.Fori(0, B - 1) as b:
                restart()
                at = At(COUNTS, b)
                attention(at, False)
                project(at, False, G1, X1)
            restart()
            at = At(COUNTS, B - 1)
            attention(at, True)
            recip(at, 3)
            scale_o(at, 3)
            for t in range(QT):
                output(at, t, X2[("out", t)])

        @block.tensor
        def _(pe):
            def g_bank(at, k):
                if k >= NG:
                    pe.wait_ge(g_evac, at("g", k - NG + 1))
                elif at.b is not None:
                    pe.wait_ge(g_evac, at("g", 0))
                return G[k % NG]

            def x_bank(at, k):
                if k >= NX:
                    pe.wait_ge(x_done, at("x", k - NX + 1))
                elif at.b is not None:
                    pe.wait_ge(x_done, at("x", 0))
                return X[k % NX]

            def project_t(at, i, u, k):
                bank = g_bank(at, k)
                ms = slice(P * (u % KT), P * (u % KT) + P)
                n = 0
                for kt in range(KT):
                    if u == KT and not rope:
                        pe.wait_ge(x_split, at("split", kt + 1))
                    for w, x in ((Wh[i], xh), (Wh[i], xl), (Wl[i], xh)):
                        last = pe.matmul(bank[:, :], w[:, kt, ms], x[:, kt, :], start=n == 0, stop=n == 3 * KT - 1)
                        n += 1
                last.then_inc(g_full, 1)
                return last

            def project_v(at, order, first, last):
                for m in range(first, last):
                    t, n = divmod(m, 3 * KT)
                    k = order[("v", t)]
                    bank = g_bank(at, k) if n == 0 else G[k % NG]
                    kt, ts = n // 3, slice(P * t, P * t + P)
                    x, w = ((xh, Wh[2]), (xh, Wl[2]), (xl, Wh[2]))[n % 3]
                    one = pe.matmul(bank[:, :], x[:, kt, ts], w[:, kt, :], start=n == 0, stop=n == 3 * KT - 1)
                    if n == 3 * KT - 1:
                        one.then_inc(g_full, 1)

            def output(at, t, k):
                bank = x_bank(at, k)
                for a in range(NGRP):
                    last = pe.matmul(bank[:, :], O[:, a, P * t:P * t + P], Wo[:, a, :], start=a == 0, stop=a == NGRP - 1)
                last.then_inc(x_full, 1)

            def max_score(at, s, qt, k):
                bank = x_bank(at, k)
                pe.matmul(bank[:, :], qstk[0:96, s, P * qt:P * qt + P], kstk[0:96, s, :],
                          start=True, stop=True).then_inc(x_full, 1)

            def max_turn(at, a, k, k_last):
                bank = x_bank(at, k)
                pe.wait_ge(x_done, at("x", k_last + 1))
                pe.transpose(bank[0:16, 0:P], mx[:, a % 2, :], ident[:, :]).then_inc(x_full, 1)

            def turn(at, t, k):
                bank = x_bank(at, k)
                pe.wait_ge(stage_in[t % 2], at("stage", 16 * (t // 2 + 1)))
                for kt in range(KT):
                    last = pe.transpose(bank[:, P * kt:P * kt + P], stage[:, t % 2, P * kt:P * kt + P], ident[:, :])
                last.then_inc(x_full, 1)

            def weighted(at, n):
                a, kt = divmod(n, KT)
                pe.wait_ge(g_evac, at("g", G1[("score", n, NC - 1)] + 1))
                if kt == 0:
                    if a:
                        pe.wait_ge(o_copied, at("group", a))
                for c in range(NC):
                    h = NC * c + a
                    last = pe.matmul(OP[32 * c:32 * c + 32, :], V[:, kt, HD * h:HD * h + HD], prob[:, n % 3, c],
                                     start=kt == 0, stop=kt == KT - 1, tile_position=(0, 32 * c))
                if kt < KT - 1:
                    last.then_inc(p_used, 1)
                    return
                last.then_inc(o_full, 1)
                if a:
                    pe.wait_ge(s_copied, at("group", a))
                for c in range(NC):
                    last = pe.matmul(SP_[32 * c:32 * c + 32, :], ones[:, :], prob[:, n % 3, c],
                                     start=True, stop=False, tile_position=(0, 32 * c))
                last.then_inc(p_used, 1)

            def sum_rest(at, g):
                pe.wait_ge(acc_added, at("acc", 8 * g + 8))
                for c in range(NC):
                    last = pe.matmul(SP_[32 * c:32 * c + 32, :], ones[:, :], acc[:, c],
                                     start=False, stop=True, tile_position=(0, 32 * c))
                last.then_inc(s_full, 1)

            def attention(at, last):
                order, xorder = G1, X2 if last else X1
                for n in range(STEPS):
                    a, kt = divmod(n, KT)
                    if kt == 0:
                        pe.wait_ge(max_rows_in, at("max_rows", 32 * a))
                    s = n + LEAD
                    for c in range(NC):
                        k = order[("score", n, c)]
                        bank = g_bank(at, k)
                        pe.matmul(bank[:, :], kstk[0:98, NC * a + c, P * kt:P * kt + P], qstk[0:98, NC * a + c, :],
                                  start=True, stop=True).then_inc(g_full, 1)
                        if s < H:
                            max_score(at, s, c, xorder[("max", s, c)])
                        if c == 1 and n in turned:
                            max_turn(at, turned[n], xorder[("mt", turned[n])], xorder[("max", s - 1, QT - 1)])
                        if c == 2 and n > 0:
                            weighted(at, n - 1)
                    if n > 4 and n % KT == 1:
                        sum_rest(at, n // KT - 1)
                    if n in (11, 12, 13, 14) and not last and not rope:
                        turn(at, n - 11, xorder[("turn", n - 11)])
                weighted(at, STEPS - 1)

            def project(at, first, order, xorder):
                if first:
                    pe.wait_ge(w_lo, 1)
                if rope:
                    pe.wait_ge(x_split, at("split", KT))
                else:
                    pe.wait_ge(x_done, at("x", xorder[("turn", QT - 1)] + 1))
                for u in range(KT):
                    last = project_t(at, 0, u, order[("q", u)])
                    if u == 0 and not first:
                        sum_rest(at, 3)
                if first:
                    pe.wait_ge(w_lo, 3)
                    pe.wait_ge(wo_in, 16)
                    if rope:
                        pe.wait_ge(bvb_ready, NGRP)
                        for a in range(NGRP):
                            last = pe.matmul(SP_[:, :], O[:, a, 0:P], Wo[:, a, :], start=a == 0, stop=a == NGRP - 1)
                        last.then_inc(bo_sum, 1)
                for u in range(KT):
                    project_t(at, 1, KT + u, order[("k", u)])
                    if u == 1 and not first:
                        pe.wait_ge(o_ready, at("group", NGRP))
                        output(at, 0, xorder[("out", 0)])
                if not first:
                    for t in range(1, QT):
                        output(at, t, xorder[("out", t)])
                before = 3 * KT if rope else 0
                within = 3 * KT * QT - before
                project_v(at, order, 0, before)
                for s in range(LEAD):
                    if s % NC == 0:
                        for half in stack_in:
                            pe.wait_ge(half[s // NC], at("stack", 96))
                    for qt in range(QT):
                        max_score(at, s, qt, xorder[("max", s, qt)])
                        if s == 4 and qt == 1:
                            max_turn(at, 0, xorder[("mt", 0)], xorder[("max", NC - 1, QT - 1)])
                        slot = QT * s + qt
                        project_v(at, order, before + within * slot // (LEAD * QT),
                                  before + within * (slot + 1) // (LEAD * QT))

            at = At(COUNTS)
            pe.wait_ge(const_ready, 6)
            if not rope:
                for t in range(4):
                    turn(at, t, X0[("turn", t)])
            project(at, True, G0, X0)
            pe.wait_ge(ones_rows, 1)
            with pe.Fori(0, B - 1) as b:
                at = At(COUNTS, b)
                attention(at, False)
                project(at, False, G1, X1)
            at = At(COUNTS, B - 1)
            attention(at, True)
            sum_rest(at, 3)
            pe.wait_ge(o_ready, at("group", NGRP))
            for t in range(QT):
                output(at, t, X2[("out", t)])


def feed_forward(nc, z, weights, out_dram, constants):
    win_d, bin_d, w1_d, b1_d, w2_d, b2_d, wout_d, bout_d = weights
    spread_d, block_d = constants

    def upto(b, each, k, ahead=0):
        return b * each + (ahead * each + k)

    ctx = ExitStack()
    with ctx:
        def sb(name, shape, dt=F32):
            return ctx.enter_context(nc.sbuf_tensor("ffn_" + name, shape, dt))

        def sem(name):
            return ctx.enter_context(nc.semaphore("ffn_" + name))

        wstage = sb("wstage", [P, KT, M])
        wostage = sb("wostage", [P, D])
        win = sb("win", [P, KT, 2 * M], F32R)
        wout_h, wout_l = sb("wout_hi", [P, D], F32R), sb("wout_lo", [P, D], F32R)
        sp_f = sb("spread_f32", [P, FT, P])
        spread = sb("spread", [P, FT, P], F32R)
        block_mask = sb("block_mask", [P, FT, M])
        w2b = sb("w2_blocks", [P, FT, M])
        w1c, b1c, w2c = sb("w1", [P, FT]), sb("b1", [P, FT]), sb("w2", [P, FT])
        b_in, b_g = sb("b_in", [P, 1]), sb("b_g", [P, 1])
        bout = sb("bout", [P, D])
        ident = sb("ident", [P, P])
        half, minus, eps = sb("neg_half", [P, QT]), sb("minus_one", [P, QT]), sb("eps", [P, QT])
        stage = sb("stage", [P, QT, D])
        zh, zl = sb("z_hi", [P, KT, S], F32R), sb("z_lo", [P, KT, S], F32R)
        s32, s_h, s_l = sb("s", [P, S]), sb("s_hi", [P, S], F32R), sb("s_lo", [P, S], F32R)
        hid = sb("hidden", [P, 4, S])
        g32, g_h, g_l = sb("g", [P, S]), sb("g_hi", [P, S], F32R), sb("g_lo", [P, S], F32R)
        res, total, normed = sb("res", [P, QT, D]), sb("total", [P, QT, D]), sb("normed", [P, QT, D])
        st, mv, lns = sb("bn_stats", [P, QT, 6]), sb("bn_mv", [P, QT, 2]), sb("ln_small", [P, 4, QT])

        G = [ctx.enter_context(nc.psum_tensor(f"fg{i}", [P, 512], F32)) for i in range(4)]
        T = [ctx.enter_context(nc.psum_tensor(f"ft{i}", [P, 512], F32)) for i in range(2)]
        SP_ = ctx.enter_context(nc.psum_tensor("f_s", [P, 512], F32))
        GP = ctx.enter_context(nc.psum_tensor("f_g", [P, 512], F32))

        small_in, big_in = sem("small_in"), sem("big_in")
        stage_in = [sem(f"stage_in{t}") for t in range(QT)]
        res_in, y_out = [sem(f"res_in{t}") for t in range(QT)], [sem(f"y_out{t}") for t in range(QT)]
        const_ready, weights_ready = sem("const_ready"), sem("weights_ready")
        t_full, t_done, s_full, s_split = sem("t_full"), sem("t_done"), sem("s_full"), sem("s_split")
        g_full, g_evac, contracted, c_split = sem("g_full"), sem("g_evac"), sem("contracted"), sem("c_split")
        o_full, bias_added, r_added = sem("o_full"), sem("bias_added"), sem("r_added")
        ln_stats, ln_small, ln_out = sem("ln_stats"), sem("ln_small"), sem("ln_out")
        dve_seq = sem("dve_seq")
        block = ctx.enter_context(nc.Block())

        @block.sync
        def _(sp):
            for t in range(QT):
                sp.dma_start(stage[:, t], z[0, t]).then_inc(stage_in[t], 16)
            for dst, src in ((wstage[:, :, :], win_d), (wostage[0:M], wout_d), (wostage[M:P], wout_d),
                             (sp_f[:, :, :], spread_d), (block_mask[:, :, :], block_d), (w2c[:, :], w2_d)):
                sp.dma_start(dst, src).then_inc(big_in, 16)
            sp.wait_ge(const_ready, 2)
            for dst, src in ((w1c[:, :], w1_d), (b1c[:, :], b1_d), (b_in[0:M], bin_d), (b_g[0:M], b2_d),
                             (bout[:, :], bout_d)):
                sp.dma_start(dst, src).then_inc(small_in, 16)

            def load_stage(b, ahead):
                for t in range(QT):
                    sp.wait_ge(t_full, upto(b, QT, t + 1, ahead - 1))
                    sp.dma_start(stage[:, t], z[b + ahead, t]).then_inc(stage_in[t], 16)

            def load_res(b):
                for t in range(QT):
                    sp.wait_ge(r_added, upto(b, QT, t + 1))
                    sp.dma_start(res[:, t], z[b + 1, t]).then_inc(res_in[t], 16)

            def store_before(b):
                for t in range(QT):
                    sp.wait_ge(ln_out, upto(b, QT, t + 1, -1))
                    sp.dma_start(out_dram[b - 1, t], normed[:, t]).then_inc(y_out[t], 16)

            for t in range(QT):
                sp.dma_start(res[:, t], z[0, t]).then_inc(res_in[t], 16)
            load_stage(0, 1)
            load_stage(0, 2)
            load_res(0)
            with sp.Fori(1, B - 2) as b:
                load_stage(b, 2)
                store_before(b)
                load_res(b)
            store_before(B - 2)
            load_res(B - 2)
            store_before(B - 1)
            store_before(B)
            for t in range(QT):
                sp.wait_ge(y_out[t], 16 * B)

        @block.gpsimd
        def _(pool):
            pool.memset(b_in[:, :], 0.0).then_inc(const_ready, 1)
            pool.memset(b_g[:, :], 0.0).then_inc(const_ready, 1)
            pool.memset(ident[:, :], 0.0).then_inc(const_ready, 1)
            pool.memset(half[:, :], -0.5).then_inc(const_ready, 1)
            pool.memset(minus[:, :], -1.0).then_inc(const_ready, 1)
            pool.memset(eps[:, :], EPS).then_inc(const_ready, 1)
            pool.wait_ge(const_ready, 6)
            pool.affine_select(out=ident[:, :], in_=ident[:, :], compare_op=ALU.not_equal, fill=1.0,
                               base=0, pattern=[[-1, P]], channel_multiplier=1).then_inc(const_ready, 1)
            pool.wait_ge(small_in, 80)

            def bias(b, ahead):
                for t in range(QT):
                    pool.wait_ge(res_in[t], upto(b, 16, 16, ahead))
                    pool.tensor_tensor(res[:, t], res[:, t], bout[:, :], ALU.add).then_inc(bias_added, 1)

            def ln_scalars(b, first):
                pool.wait_ge(ln_stats, upto(b, QT, QT))
                if not first:
                    pool.wait_ge(ln_out, upto(b, QT, 0))
                pool.tensor_tensor(lns[:, 0], mv[:, :, 1], eps[:, :], ALU.add).then_inc(ln_small, 1)
                pool.tensor_tensor(lns[:, 1], mv[:, :, 0], minus[:, :], ALU.mult).then_inc(ln_small, 1)
                pool.wait_ge(ln_small, upto(b, 4, 2))
                pool.tensor_tensor(lns[:, 2], lns[:, 0], half[:, :], ALU.pow).then_inc(ln_small, 1)
                pool.wait_ge(ln_small, upto(b, 4, 3))
                pool.tensor_tensor(lns[:, 3], lns[:, 1], lns[:, 2], ALU.mult).then_inc(ln_small, 1)

            bias(0, 0)
            ln_scalars(0, True)
            with pool.Fori(1, B) as b:
                bias(b, 0)
                ln_scalars(b, False)

        @block.scalar
        def _(act):
            act.wait_ge(small_in, 80)

            def inner(b):
                for f in range(FT):
                    act.wait_ge(g_full, upto(b, FT, f + 1))
                    if f >= 4:
                        act.wait_ge(contracted, upto(b, FT, f - 3))
                    act.activation(hid[:, f % 4], G[f % 4][:, :], ACT.Relu, bias=b1c[:, f:f + 1],
                                   scale=w1c[:, f:f + 1]).then_inc(g_evac, 1)

            def normalise_before(b, stored):
                for t in range(QT):
                    act.wait_ge(ln_small, upto(b, 4, 0))
                    if stored:
                        act.wait_ge(y_out[t], upto(b, 16, -16))
                    act.activation(normed[:, t], total[:, t], ACT.Identity, bias=lns[:, 3, t:t + 1],
                                   scale=lns[:, 2, t:t + 1]).then_inc(ln_out, 1)

            inner(0)
            inner(1)
            normalise_before(1, False)
            with act.Fori(2, B) as b:
                inner(b)
                normalise_before(b, True)
            normalise_before(B, True)

        @block.vector
        def _(dve):
            seq = [0]

            def link(ins):
                ins.then_inc(dve_seq, 1)
                seq[0] += 1
                dve.wait_ge(dve_seq, seq[0])

            def restart():
                dve.sem_clear(dve_seq)
                seq[0] = 0

            def split(b, ahead, tiles):
                for t in tiles:
                    dve.wait_ge(t_full, upto(b, QT, t + 1, ahead))
                    src = T[t % 2][:, :].rearrange("p (k t) -> p k t", k=KT)
                    hi, lo = zh[:, :, P * t:P * t + P], zl[:, :, P * t:P * t + P]
                    link(dve.tensor_copy(hi, src))
                    dve.tensor_tensor(lo, src, hi, ALU.subtract).then_inc(t_done, 1)

            def units(b, ahead):
                dve.wait_ge(s_full, upto(b, 1, 1, ahead))
                link(dve.tensor_scalar(s32[:, :], SP_[:, :], b_in[:, 0:1], None, ALU.add))
                link(dve.tensor_copy(s_h[:, :], s32[:, :]))
                dve.tensor_tensor(s_l[:, :], s32[:, :], s_h[:, :], ALU.subtract).then_inc(s_split, 1)

            def contraction(b):
                dve.wait_ge(contracted, upto(b, FT, FT))
                link(dve.tensor_scalar(g32[:, :], GP[:, :], b_g[:, 0:1], None, ALU.add))
                link(dve.tensor_copy(g_h[:, :], g32[:, :]))
                dve.tensor_tensor(g_l[:, :], g32[:, :], g_h[:, :], ALU.subtract).then_inc(c_split, 1)

            def output(b, first):
                for t in range(QT):
                    dve.wait_ge(o_full, upto(b, QT, t + 1))
                    dve.wait_ge(bias_added, upto(b, QT, t + 1))
                    if not first:
                        dve.wait_ge(ln_out, upto(b, QT, t + 1, -1))
                    dve.tensor_tensor(total[:, t], G[t][:, :], res[:, t], ALU.add).then_inc(r_added, 1)

            def stats_before(b):
                for t in range(QT):
                    dve.wait_ge(r_added, upto(b, QT, t + 1, -1))
                    link(dve.bn_stats(st[:, t], total[:, t]))
                    dve.bn_aggr(mv[:, t], st[:, t]).then_inc(ln_stats, 1)

            def batch(b, first):
                split(b, 1, (0, 1))
                if not first:
                    stats_before(b)
                split(b, 1, (2, 3))
                contraction(b)
                units(b, 1)
                output(b, first)

            dve.wait_ge(big_in, 96)
            dve.tensor_copy(win[:, :, 0:M], wstage[:, :, :]).then_inc(weights_ready, 1)
            dve.tensor_copy(wout_h[:, :], wostage[:, :]).then_inc(weights_ready, 1)
            dve.wait_ge(weights_ready, 2)
            dve.tensor_tensor(win[:, :, M:2 * M], wstage[:, :, :], win[:, :, 0:M], ALU.subtract).then_inc(weights_ready, 1)
            dve.tensor_tensor(wout_l[:, :], wostage[:, :], wout_h[:, :], ALU.subtract).then_inc(weights_ready, 1)
            split(0, 0, range(QT))
            dve.tensor_copy(spread[:, :, :], sp_f[:, :, :]).then_inc(weights_ready, 1)
            for f in range(FT):
                dve.tensor_scalar(w2b[:, f], block_mask[:, f], w2c[:, f:f + 1], None, ALU.mult).then_inc(weights_ready, 1)
            dve.wait_ge(small_in, 80)
            units(0, 0)
            batch(0, True)
            with dve.Fori(1, B - 1) as b:
                restart()
                batch(b, False)
            restart()
            stats_before(B - 1)
            contraction(B - 1)
            output(B - 1, False)
            stats_before(B)

        @block.tensor
        def _(pe):
            def turn(b, t, ahead, first):
                pe.wait_ge(stage_in[t], upto(b, 16, 16, ahead))
                if t >= 2 or not first:
                    pe.wait_ge(t_done, upto(b, QT, t - 1, ahead))
                for kt in range(KT):
                    last = pe.transpose(T[t % 2][:, P * kt:P * kt + P], stage[:, t, P * kt:P * kt + P], ident[:, :])
                last.then_inc(t_full, 1)

            def units(b, ahead):
                pe.wait_ge(t_done, upto(b, QT, QT, ahead))
                n = 0
                for kt in range(KT):
                    for x in (zh, zl):
                        last = pe.matmul(SP_[:, :], win[:, kt, :], x[:, kt, :], start=n == 0, stop=n == 2 * KT - 1)
                        n += 1
                last.then_inc(s_full, 1)

            def contract(b, f):
                pe.wait_ge(g_evac, upto(b, FT, f + 1))
                c = M * (f % 2)
                pe.matmul(GP[c:c + M, :], w2b[:, f, :], hid[:, f % 4], start=f < 2, stop=f >= FT - 2,
                          tile_position=(0, c)).then_inc(contracted, 1)

            def inner(b, first, last_batch):
                pe.wait_ge(s_split, upto(b, 1, 1))
                for f in range(FT):
                    if f >= 4:
                        pe.wait_ge(g_evac, upto(b, FT, f - 3))
                    elif not first:
                        pe.wait_ge(r_added, upto(b, QT, f + 1, -1))
                    for n, x in enumerate((s_h, s_l)):
                        last = pe.matmul(G[f % 4][:, :], spread[:, f, :], x[:, :], start=n == 0, stop=n == 1)
                    last.then_inc(g_full, 1)
                    if f % 2:
                        if not last_batch:
                            turn(b, f // 2, 1, False)
                        if f >= 3:
                            contract(b, f - 3)
                            contract(b, f - 2)
                contract(b, FT - 2)
                contract(b, FT - 1)

            def output(b):
                pe.wait_ge(c_split, upto(b, 1, 1))
                for t in range(QT):
                    ts = slice(P * t, P * t + P)
                    for n, (x, w) in enumerate(((g_h, wout_h), (g_h, wout_l), (g_l, wout_h))):
                        last = pe.matmul(G[t][:, :], x[:, ts], w[:, :], start=n == 0, stop=n == 2)
                    last.then_inc(o_full, 1)

            def batch(b, first):
                inner(b, first, False)
                units(b, 1)
                output(b)

            pe.wait_ge(const_ready, 7)
            for t in range(QT):
                turn(0, t, 0, True)
            pe.wait_ge(weights_ready, 4)
            units(0, 0)
            pe.wait_ge(weights_ready, 5 + FT)
            batch(0, True)
            with pe.Fori(1, B - 1) as b:
                batch(b, False)
            inner(B - 1, False, True)
            output(B - 1)


def program(nc, t):
    scratch = {n: nc.dram_tensor(n, (B, QT, P, D), F32, kind="Internal").ap() for n in ("y_scratch", "z_scratch")}
    sums = nc.dram_tensor("sums_scratch", (NGRP, NC, S), F32, kind="Internal").ap()
    attention_layer(nc, True, t["xT"], None, t["x"],
                    (t["a_wq"], t["a_wk"], t["a_wv"], t["a_wo"], t["a_bq"], t["a_bk"], t["a_bv"],
                     bass.AP(t["a_bo"].tensor, 0, [[0, P], [1, D]]), t["rotary"]),
                    scratch["y_scratch"], sums)
    attention_layer(nc, False, scratch["y_scratch"], t["ctxT"], scratch["y_scratch"],
                    (t["c_wq"], t["c_wk"], t["c_wv"], t["c_wo"], None, None, None, None, None),
                    scratch["z_scratch"], sums)
    feed_forward(nc, scratch["z_scratch"],
                 (t["f_win"], t["f_bin"], t["f_w1"], t["f_b1"], t["f_w2"], t["f_b2"], t["f_wout"],
                  bass.AP(t["f_bout"].tensor, 0, [[0, P], [1, D]])),
                 t["out"], (t["spread"], t["blocks"]))


def rotary_table():
    f = np.float32
    inv = f(1.0) / np.power(f(10000.0), np.arange(0, D, 2, dtype=f) / f(D), dtype=f)
    ang = (inv[:, None] * np.arange(S, dtype=f)[None, :]).astype(f)
    cos, sin = np.repeat(np.cos(ang), 2, 0), np.repeat(np.sin(ang), 2, 0)
    sin[0::2] *= f(-1.0)
    return np.ascontiguousarray(np.stack([cos, sin], 1).reshape(KT, P, 2, S).astype(f))


def spread_and_blocks():
    unit = (np.arange(FT)[:, None] * P + np.arange(P)[None, :]) // INNER
    spread = (np.arange(P)[:, None, None] % M == unit[None]).astype(np.float32)
    blocks = (unit.T[:, :, None] == np.arange(M)[None, None]).astype(np.float32)
    return np.ascontiguousarray(spread), np.ascontiguousarray(blocks)


def kernel(**inputs):
    import concourse.bacc as bacc
    from concourse.bass_utils import run_bass_kernel_spmd

    a = {k: np.asarray(v) for k, v in inputs.items()}

    def rows(w):
        return np.ascontiguousarray(w.reshape(KT, P, -1).transpose(1, 0, 2))

    def grouped(w):
        return np.ascontiguousarray(w.reshape(NC, NGRP, HD, -1).transpose(0, 2, 1, 3).reshape(P, NGRP, -1))

    def column(b):
        return np.ascontiguousarray(b.reshape(KT, P).T)

    spread, blocks = spread_and_blocks()
    arrays = {
        "x": a["x"].reshape(B, QT, P, D),
        "xT": np.ascontiguousarray(a["x"].transpose(0, 2, 1)).reshape(B, KT, P, S),
        "ctxT": np.ascontiguousarray(a["ctx_1024"].transpose(0, 2, 1).reshape(B, KT, P, S).transpose(0, 2, 1, 3)),
        "a_wq": rows(a["L0_attn_Wq"]), "a_wk": rows(a["L0_attn_Wk"]), "a_wv": rows(a["L0_attn_Wv"]),
        "a_wo": grouped(a["L0_attn_W0"]), "a_bq": column(a["L0_attn_bq"]), "a_bk": column(a["L0_attn_bk"]),
        "a_bv": np.ascontiguousarray(grouped(a["L0_attn_bv"][:, None])[:, :, 0]),
        "a_bo": a["L0_attn_b0"].reshape(1, D), "rotary": rotary_table(),
        "c_wq": rows(a["L0_xattn_Wq"].T), "c_wk": rows(a["L0_xattn_Wk"].T), "c_wv": rows(a["L0_xattn_Wv"].T),
        "c_wo": grouped(a["L0_xattn_Wo"].T),
        "f_win": rows(a["L0_ffn_Win"]), "f_bin": a["L0_ffn_bin_"].reshape(M, 1),
        "f_w1": np.ascontiguousarray(a["L0_ffn_W1"].reshape(FT, P).T),
        "f_b1": np.ascontiguousarray(a["L0_ffn_b1"].reshape(FT, P).T),
        "f_w2": np.ascontiguousarray(a["L0_ffn_W2"].reshape(FT, P).T), "f_b2": a["L0_ffn_b2"].reshape(M, 1),
        "f_wout": np.ascontiguousarray(a["L0_ffn_Wout"]), "f_bout": a["L0_ffn_bout"].reshape(1, D),
        "spread": spread, "blocks": blocks,
    }
    nc = bacc.Bacc("TRN2", target_bir_lowering=False, num_devices=1)
    t = {n: nc.dram_tensor(n, v.shape, F32, kind="ExternalInput").ap() for n, v in arrays.items()}
    t["out"] = nc.dram_tensor("out", (B, QT, P, D), F32, kind="ExternalOutput").ap()
    program(nc, t)
    r = run_bass_kernel_spmd(nc, [arrays], core_ids=[0])
    return r.results[0]["out"].reshape(B, S, D)
```
